# Optimizing a Trainium2 kernel written in Bass

```python
import numpy as np
import jax
import jax.numpy as jnp

def _softmax(x, axis=-1):
    return jax.nn.softmax(x, axis=axis)

def _gelu(x):
    return jax.nn.gelu(x, approximate=True)

def _silu(x):
    return jax.nn.silu(x)

def _sigmoid(x):
    return jax.nn.sigmoid(x)

def _layernorm(x, axis=-1, eps=1e-05):
    m = jnp.mean(x, axis=axis, keepdims=True)
    v = jnp.var(x, axis=axis, keepdims=True)
    return (x - m) / jnp.sqrt(v + eps)

def _scatter_add(tgt, idx, src, axis=0):
    return tgt.at[idx].add(src)

def _segment_sum(src, seg, n):
    return jax.ops.segment_sum(src, seg, n)
kernel_name = 'mk_seq_preln_d2_jaxref_r8_7bec94'

def setup_inputs(seed: int=0):
    np.random.seed(seed)
    _w = jnp.asarray

    def _L0_attn_setup():
        import jax, jax.numpy as jnp
        import numpy as np
        DIM = 256
        N_HEADS = 16
        HEAD_DIM = DIM // N_HEADS
        B, T = (2, 512)
        K_CONV = 4
        EPS = 1e-05

        def _silu(x):
            return x * jax.nn.sigmoid(x)

        def _l2norm(x):
            return x * jax.lax.rsqrt(jnp.sum(x * x, axis=-1, keepdims=True) + 1e-06)

        def _short_conv(x, w):
            K = w.shape[1]
            xp = jnp.pad(x, ((0, 0), (K - 1, 0), (0, 0)))
            y = xp[:, 0:x.shape[1], :] * w[:, 0]
            for i in range(1, K):
                y = y + xp[:, i:i + x.shape[1], :] * w[:, i]
            return _silu(y)

        def _delta_rule(q, k, v, beta):
            Dk = q.shape[-1]
            q = _l2norm(q) * Dk ** (-0.5)
            k = _l2norm(k)
            qT = jnp.swapaxes(q, 0, 1)
            kT = jnp.swapaxes(k, 0, 1)
            vT = jnp.swapaxes(v, 0, 1)
            bT = jnp.swapaxes(beta, 0, 1)

            def step(S, inp):
                qt, kt, vt, bt = inp
                u = vt - jnp.einsum('bhk,bhkv->bhv', kt, S)
                S = S + bt[:, :, None, None] * kt[..., :, None] * u[..., None, :]
                o = jnp.einsum('bhk,bhkv->bhv', qt, S)
                return (S, o)
            S0 = jnp.zeros(q.shape[0:1] + q.shape[2:4] + (v.shape[-1],), dtype=q.dtype)
            _, o = jax.lax.scan(step, S0, (qT, kT, vT, bT))
            return jnp.swapaxes(o, 0, 1)

        def _rmsnorm(x, w):
            var = jnp.mean(x * x, axis=-1, keepdims=True)
            return x * jax.lax.rsqrt(var + EPS) * w
        key = jax.random.key(seed)
        ks = jax.random.split(key, 16)
        std = 0.02
        inp = {'hidden_states': jax.random.normal(ks[0], (B, T, DIM), jnp.float32), 'k_cache': jax.random.normal(ks[1], (B, T, N_HEADS, HEAD_DIM), jnp.float32), 'v_cache': jax.random.normal(ks[2], (B, T, N_HEADS, HEAD_DIM), jnp.float32), 'cos': jax.random.normal(ks[3], (B, T, HEAD_DIM), jnp.float32), 'sin': jax.random.normal(ks[4], (B, T, HEAD_DIM), jnp.float32), 'Wq': jax.random.normal(ks[5], (DIM, DIM), jnp.float32) * std, 'Wk': jax.random.normal(ks[6], (DIM, DIM), jnp.float32) * std, 'Wv': jax.random.normal(ks[7], (DIM, DIM), jnp.float32) * std, 'Wo': jax.random.normal(ks[8], (DIM, DIM), jnp.float32) * std, 'Wg': jax.random.normal(ks[9], (DIM, DIM), jnp.float32) * std, 'Wb': jax.random.normal(ks[10], (DIM, N_HEADS), jnp.float32) * std, 'conv_wq': jax.random.normal(ks[11], (DIM, K_CONV), jnp.float32) * 0.3, 'conv_wk': jax.random.normal(ks[12], (DIM, K_CONV), jnp.float32) * 0.3, 'conv_wv': jax.random.normal(ks[13], (DIM, K_CONV), jnp.float32) * 0.3, 'norm_w': jnp.ones((HEAD_DIM,), jnp.float32)}
        return inp
    _L0_attn_in = _L0_attn_setup()

    def _L0_ffn_setup():
        import jax, jax.numpy as jnp
        import numpy as np
        B, T, C = (2, 128, 256)
        E, TOPK = (8, 2)
        F_MOE = 176
        F_SHARED = 704
        key = jax.random.key(seed)
        ks = jax.random.split(key, 9)
        s = 0.02
        return {'x': jax.random.normal(ks[0], (B, T, C), dtype=jnp.float32), 'gate_w': jax.random.normal(ks[1], (E, C), dtype=jnp.float32) * s, 'expert_fc1': jax.random.normal(ks[2], (E, F_MOE, C), dtype=jnp.float32) * s, 'expert_fc2': jax.random.normal(ks[3], (E, F_MOE, C), dtype=jnp.float32) * s, 'expert_proj': jax.random.normal(ks[4], (E, C, F_MOE), dtype=jnp.float32) * s, 'shared_fc1': jax.random.normal(ks[5], (F_SHARED, C), dtype=jnp.float32) * s, 'shared_fc2': jax.random.normal(ks[6], (F_SHARED, C), dtype=jnp.float32) * s, 'shared_proj': jax.random.normal(ks[7], (C, F_SHARED), dtype=jnp.float32) * s, 'shared_gate_w': jax.random.normal(ks[8], (1, C), dtype=jnp.float32) * s}
    _L0_ffn_in = _L0_ffn_setup()

    def _L1_attn_setup():
        import jax, jax.numpy as jnp
        import numpy as np
        HIDDEN = 256
        N_HEADS = 16
        N_KV_HEADS = 2
        HEAD_DIM = 128
        THETA = 10000.0
        SCALE = 0.08838834764831845
        SOFTCAP = 30.0

        def apply_rotary_emb(x, theta=THETA):
            B, S, H, D = x.shape
            inv_freq = 1.0 / theta ** (jnp.arange(0, D, 2, dtype=jnp.float32) / D)
            t = jnp.arange(S, dtype=jnp.float32)
            freqs = jnp.outer(t, inv_freq)
            cos = jnp.cos(freqs)[None, :, None, :]
            sin = jnp.sin(freqs)[None, :, None, :]
            x1, x2 = (x[..., :D // 2], x[..., D // 2:])
            out = jnp.concatenate([x1 * cos - x2 * sin, x1 * sin + x2 * cos], axis=-1)
            return out.astype(x.dtype)
        key = jax.random.key(seed)
        k1, k2, k3 = jax.random.split(key, 3)
        B, S = (2, 256)
        qkv_out = (N_HEADS + 2 * N_KV_HEADS) * HEAD_DIM
        hidden_states = jax.random.normal(k1, (B, S, HIDDEN), dtype=jnp.float32)
        Wqkv = jax.random.normal(k2, (HIDDEN, qkv_out), dtype=jnp.float32) * HIDDEN ** (-0.5)
        Wo = jax.random.normal(k3, (N_HEADS * HEAD_DIM, HIDDEN), dtype=jnp.float32) * (N_HEADS * HEAD_DIM) ** (-0.5)
        return {'hidden_states': hidden_states, 'Wqkv': Wqkv, 'Wo': Wo}
    _L1_attn_in = _L1_attn_setup()

    def _L1_ffn_setup():
        import jax, jax.numpy as jnp
        import numpy as np
        B, S, D = (2, 256, 256)
        MOE_D = 176
        E = 16
        K = 6
        ALPHA = 0.001

        def _moe_forward(x, gate_w, w_gate, w_up, w_down):
            b, s, d = x.shape
            T = b * s
            h = x.reshape(T, d)
            logits = h @ gate_w.T
            scores = jax.nn.softmax(logits.astype(jnp.float32), axis=-1)
            topk_w, topk_idx = jax.lax.top_k(scores, K)
            cw = jnp.zeros((T, E), jnp.float32)
            cw = cw.at[jnp.arange(T)[:, None], topk_idx].add(topk_w)
            y = jnp.zeros((T, d), x.dtype)
            for e in range(E):
                g = h @ w_gate[e].T
                u = h @ w_up[e].T
                out = jax.nn.silu(g) * u @ w_down[e].T
                y = y + cw[:, e:e + 1].astype(x.dtype) * out
            counts = jnp.sum(jax.nn.one_hot(topk_idx.reshape(b, s * K), E, dtype=jnp.float32), axis=1)
            ce = counts * (E / (s * K))
            scores_bse = scores.reshape(b, s, E)
            aux = jnp.mean(jnp.sum(ce * scores_bse.mean(axis=1), axis=1)) * ALPHA
            return (y.reshape(b, s, d), aux)
        key = jax.random.key(seed)
        ks = jax.random.split(key, 5)
        sd = 1.0 / np.sqrt(D)
        sm = 1.0 / np.sqrt(MOE_D)
        return {'x': jax.random.normal(ks[0], (B, S, D), jnp.float32), 'gate_w': jax.random.normal(ks[1], (E, D), jnp.float32) * sd, 'w_gate': jax.random.normal(ks[2], (E, MOE_D, D), jnp.float32) * sd, 'w_up': jax.random.normal(ks[3], (E, MOE_D, D), jnp.float32) * sd, 'w_down': jax.random.normal(ks[4], (E, D, MOE_D), jnp.float32) * sm}
    _L1_ffn_in = _L1_ffn_setup()
    _d = {'L0_attn_hidden_states': _L0_attn_in['hidden_states'], 'L0_attn_k_cache': _L0_attn_in['k_cache'], 'L0_attn_v_cache': _L0_attn_in['v_cache'], 'L0_attn_cos': _L0_attn_in['cos'], 'L0_attn_sin': _L0_attn_in['sin'], 'L0_attn_Wq': _L0_attn_in['Wq'], 'L0_attn_Wk': _L0_attn_in['Wk'], 'L0_attn_Wv': _L0_attn_in['Wv'], 'L0_attn_Wo': _L0_attn_in['Wo'], 'L0_attn_Wg': _L0_attn_in['Wg'], 'L0_attn_Wb': _L0_attn_in['Wb'], 'L0_attn_conv_wq': _L0_attn_in['conv_wq'], 'L0_attn_conv_wk': _L0_attn_in['conv_wk'], 'L0_attn_conv_wv': _L0_attn_in['conv_wv'], 'L0_attn_norm_w': _L0_attn_in['norm_w'], 'L0_ffn_gate_w': _L0_ffn_in['gate_w'], 'L0_ffn_expert_fc1': _L0_ffn_in['expert_fc1'], 'L0_ffn_expert_fc2': _L0_ffn_in['expert_fc2'], 'L0_ffn_expert_proj': _L0_ffn_in['expert_proj'], 'L0_ffn_shared_fc1': _L0_ffn_in['shared_fc1'], 'L0_ffn_shared_fc2': _L0_ffn_in['shared_fc2'], 'L0_ffn_shared_proj': _L0_ffn_in['shared_proj'], 'L0_ffn_shared_gate_w': _L0_ffn_in['shared_gate_w'], 'L1_attn_Wqkv': _L1_attn_in['Wqkv'], 'L1_attn_Wo': _L1_attn_in['Wo'], 'L1_ffn_gate_w': _L1_ffn_in['gate_w'], 'L1_ffn_w_gate': _L1_ffn_in['w_gate'], 'L1_ffn_w_up': _L1_ffn_in['w_up'], 'L1_ffn_w_down': _L1_ffn_in['w_down']}
    _x0 = _d['L0_attn_hidden_states']
    _d['L0_attn_hidden_states'] = jax.random.normal(jax.random.fold_in(jax.random.key(seed), 1), (2, 512, 256), dtype=_x0.dtype)
    del _x0
    return _d

def reference(L0_attn_hidden_states, L0_attn_k_cache, L0_attn_v_cache, L0_attn_cos, L0_attn_sin, L0_attn_Wq, L0_attn_Wk, L0_attn_Wv, L0_attn_Wo, L0_attn_Wg, L0_attn_Wb, L0_attn_conv_wq, L0_attn_conv_wk, L0_attn_conv_wv, L0_attn_norm_w, L0_ffn_gate_w, L0_ffn_expert_fc1, L0_ffn_expert_fc2, L0_ffn_expert_proj, L0_ffn_shared_fc1, L0_ffn_shared_fc2, L0_ffn_shared_proj, L0_ffn_shared_gate_w, L1_attn_Wqkv, L1_attn_Wo, L1_ffn_gate_w, L1_ffn_w_gate, L1_ffn_w_up, L1_ffn_w_down):

    def _L0_attn_ref(hidden_states, k_cache, v_cache, cos, sin, Wq, Wk, Wv, Wo, Wg, Wb, conv_wq, conv_wk, conv_wv, norm_w):
        import jax, jax.numpy as jnp
        import numpy as np
        DIM = 256
        N_HEADS = 16
        HEAD_DIM = DIM // N_HEADS
        B, T = (2, 512)
        K_CONV = 4
        EPS = 1e-05

        def _silu(x):
            return x * jax.nn.sigmoid(x)

        def _l2norm(x):
            return x * jax.lax.rsqrt(jnp.sum(x * x, axis=-1, keepdims=True) + 1e-06)

        def _short_conv(x, w):
            K = w.shape[1]
            xp = jnp.pad(x, ((0, 0), (K - 1, 0), (0, 0)))
            y = xp[:, 0:x.shape[1], :] * w[:, 0]
            for i in range(1, K):
                y = y + xp[:, i:i + x.shape[1], :] * w[:, i]
            return _silu(y)

        def _delta_rule(q, k, v, beta):
            Dk = q.shape[-1]
            q = _l2norm(q) * Dk ** (-0.5)
            k = _l2norm(k)
            qT = jnp.swapaxes(q, 0, 1)
            kT = jnp.swapaxes(k, 0, 1)
            vT = jnp.swapaxes(v, 0, 1)
            bT = jnp.swapaxes(beta, 0, 1)

            def step(S, inp):
                qt, kt, vt, bt = inp
                u = vt - jnp.einsum('bhk,bhkv->bhv', kt, S)
                S = S + bt[:, :, None, None] * kt[..., :, None] * u[..., None, :]
                o = jnp.einsum('bhk,bhkv->bhv', qt, S)
                return (S, o)
            S0 = jnp.zeros(q.shape[0:1] + q.shape[2:4] + (v.shape[-1],), dtype=q.dtype)
            _, o = jax.lax.scan(step, S0, (qT, kT, vT, bT))
            return jnp.swapaxes(o, 0, 1)

        def _rmsnorm(x, w):
            var = jnp.mean(x * x, axis=-1, keepdims=True)
            return x * jax.lax.rsqrt(var + EPS) * w
        b, t, d = hidden_states.shape
        q = hidden_states @ Wq
        k = hidden_states @ Wk
        v = hidden_states @ Wv
        q = _short_conv(q, conv_wq)
        k = _short_conv(k, conv_wk)
        v = _short_conv(v, conv_wv)
        q = q.reshape(b, t, N_HEADS, HEAD_DIM)
        k = k.reshape(b, t, N_HEADS, HEAD_DIM)
        v = v.reshape(b, t, N_HEADS, HEAD_DIM)
        beta = jax.nn.sigmoid(hidden_states @ Wb)
        o = _delta_rule(q, k, v, beta)
        o = _rmsnorm(o, norm_w)
        g = (hidden_states @ Wg).reshape(b, t, N_HEADS, HEAD_DIM)
        o = o * jax.nn.sigmoid(g)
        o = o.reshape(b, t, d) @ Wo
        return o

    def _L0_ffn_ref(x, gate_w, expert_fc1, expert_fc2, expert_proj, shared_fc1, shared_fc2, shared_proj, shared_gate_w):
        import jax, jax.numpy as jnp
        import numpy as np
        B, T, C = (2, 128, 256)
        E, TOPK = (8, 2)
        F_MOE = 176
        F_SHARED = 704
        b, t, c = x.shape
        xf = x.reshape(-1, c)
        n = xf.shape[0]
        router = xf @ gate_w.T
        probs = jax.nn.softmax(router.astype(jnp.float32), axis=1).astype(x.dtype)
        top_p, top_i = jax.lax.top_k(probs, TOPK)
        combine = jnp.zeros((n, E), dtype=x.dtype).at[jnp.arange(n)[:, None], top_i].set(top_p)
        h1 = jnp.einsum('nc,efc->enf', xf, expert_fc1)
        h2 = jnp.einsum('nc,efc->enf', xf, expert_fc2)
        h = jax.nn.silu(h1) * h2
        out_e = jnp.einsum('enf,ecf->enc', h, expert_proj)
        y = jnp.einsum('ne,enc->nc', combine, out_e)
        s1 = xf @ shared_fc1.T
        s2 = xf @ shared_fc2.T
        shared = jax.nn.silu(s1) * s2 @ shared_proj.T
        y = y + jax.nn.sigmoid(xf @ shared_gate_w.T) * shared
        return y.reshape(b, t, c)

    def _L1_attn_ref(hidden_states, Wqkv, Wo):
        import jax, jax.numpy as jnp
        import numpy as np
        HIDDEN = 256
        N_HEADS = 16
        N_KV_HEADS = 2
        HEAD_DIM = 128
        THETA = 10000.0
        SCALE = 0.08838834764831845
        SOFTCAP = 30.0

        def apply_rotary_emb(x, theta=THETA):
            B, S, H, D = x.shape
            inv_freq = 1.0 / theta ** (jnp.arange(0, D, 2, dtype=jnp.float32) / D)
            t = jnp.arange(S, dtype=jnp.float32)
            freqs = jnp.outer(t, inv_freq)
            cos = jnp.cos(freqs)[None, :, None, :]
            sin = jnp.sin(freqs)[None, :, None, :]
            x1, x2 = (x[..., :D // 2], x[..., D // 2:])
            out = jnp.concatenate([x1 * cos - x2 * sin, x1 * sin + x2 * cos], axis=-1)
            return out.astype(x.dtype)
        B, S, _ = hidden_states.shape
        q_size = N_HEADS * HEAD_DIM
        kv_size = N_KV_HEADS * HEAD_DIM
        qkv = hidden_states @ Wqkv
        xq = qkv[..., :q_size].reshape(B, S, N_HEADS, HEAD_DIM)
        xk = qkv[..., q_size:q_size + kv_size].reshape(B, S, N_KV_HEADS, HEAD_DIM)
        xv = qkv[..., q_size + kv_size:].reshape(B, S, N_KV_HEADS, HEAD_DIM)
        xq = apply_rotary_emb(xq)
        xk = apply_rotary_emb(xk)
        rep = N_HEADS // N_KV_HEADS
        xk = jnp.repeat(xk, rep, axis=2)
        xv = jnp.repeat(xv, rep, axis=2)
        logits = jnp.einsum('bqhd,bkhd->bhqk', xq, xk) * SCALE
        logits = SOFTCAP * jnp.tanh(logits / SOFTCAP)
        causal = jnp.tril(jnp.ones((S, S), dtype=bool))
        logits = jnp.where(causal[None, None], logits, jnp.float32(-1e+30))
        scores = jax.nn.softmax(logits, axis=-1)
        out = jnp.einsum('bhqk,bkhd->bqhd', scores, xv).reshape(B, S, N_HEADS * HEAD_DIM)
        return out @ Wo

    def _L1_ffn_ref(x, gate_w, w_gate, w_up, w_down):
        import jax, jax.numpy as jnp
        import numpy as np
        B, S, D = (2, 256, 256)
        MOE_D = 176
        E = 16
        K = 6
        ALPHA = 0.001

        def _moe_forward(x, gate_w, w_gate, w_up, w_down):
            b, s, d = x.shape
            T = b * s
            h = x.reshape(T, d)
            logits = h @ gate_w.T
            scores = jax.nn.softmax(logits.astype(jnp.float32), axis=-1)
            topk_w, topk_idx = jax.lax.top_k(scores, K)
            cw = jnp.zeros((T, E), jnp.float32)
            cw = cw.at[jnp.arange(T)[:, None], topk_idx].add(topk_w)
            y = jnp.zeros((T, d), x.dtype)
            for e in range(E):
                g = h @ w_gate[e].T
                u = h @ w_up[e].T
                out = jax.nn.silu(g) * u @ w_down[e].T
                y = y + cw[:, e:e + 1].astype(x.dtype) * out
            counts = jnp.sum(jax.nn.one_hot(topk_idx.reshape(b, s * K), E, dtype=jnp.float32), axis=1)
            ce = counts * (E / (s * K))
            scores_bse = scores.reshape(b, s, E)
            aux = jnp.mean(jnp.sum(ce * scores_bse.mean(axis=1), axis=1)) * ALPHA
            return (y.reshape(b, s, d), aux)
        y, _aux = _moe_forward(x, gate_w, w_gate, w_up, w_down)
        return y
    x = L0_attn_hidden_states
    x = x + _L0_attn_ref(_layernorm(x, axis=-1), L0_attn_k_cache, L0_attn_v_cache, L0_attn_cos, L0_attn_sin, L0_attn_Wq, L0_attn_Wk, L0_attn_Wv, L0_attn_Wo, L0_attn_Wg, L0_attn_Wb, L0_attn_conv_wq, L0_attn_conv_wk, L0_attn_conv_wv, L0_attn_norm_w)
    x = x + _L0_ffn_ref(_layernorm(x, axis=-1), L0_ffn_gate_w, L0_ffn_expert_fc1, L0_ffn_expert_fc2, L0_ffn_expert_proj, L0_ffn_shared_fc1, L0_ffn_shared_fc2, L0_ffn_shared_proj, L0_ffn_shared_gate_w)
    x = x + _L1_attn_ref(_layernorm(x, axis=-1), L1_attn_Wqkv, L1_attn_Wo)
    x = x + _L1_ffn_ref(_layernorm(x, axis=-1), L1_ffn_gate_w, L1_ffn_w_gate, L1_ffn_w_up, L1_ffn_w_down)
    return x

_drawn_inputs = setup_inputs


def setup_inputs(seed=0):
    import zlib

    import numpy as np

    out = dict(_drawn_inputs(seed))
    spreads = {'L0_attn_norm_w': (1.0, 0.2)}
    factors = {'L0_ffn_gate_w': 8.0,
     'L0_ffn_expert_fc1': 8.0,
     'L0_ffn_expert_fc2': 8.0,
     'L0_ffn_expert_proj': 8.0,
     'L0_ffn_shared_fc1': 3.326,
     'L0_ffn_shared_fc2': 3.279,
     'L0_ffn_shared_proj': 3.285,
     'L0_ffn_shared_gate_w': 8.0}
    for name, (base, spread) in spreads.items():
        noise = np.random.default_rng([zlib.crc32(name.encode()), seed]).standard_normal(out[name].shape)
        drawn = base * np.exp(spread * noise) if base else spread * noise
        out[name] = jnp.asarray(drawn.astype(out[name].dtype))
    for name, factor in factors.items():
        out[name] = (out[name] * factor).astype(out[name].dtype)
    return out
```

```python
from contextlib import ExitStack

import numpy as np

import concourse.bass as bass
from concourse import mybir

P = 128
BATCH, SEQ, DIM = 2, 512, 256
TOK = BATCH * SEQ
NT = TOK // P
KD = DIM // P
HALF = TOK // 2
EPS = 1e-5

H0, D0, CONV = 16, 16, 4
CH = 16
NCH = SEQ // CH
HH = P // D0
NU = KD * BATCH * NCH
NG = KD * BATCH
L2_EPS = 1e-6

HQ, HKV, DH = 16, 2, 128
REP = HQ // HKV
THETA = 10000.0
SCALE = 0.08838834764831845
SOFTCAP = 30.0
KT = SEQ // P
P_OFF = [0, 512, 1024, 896]
P_ALL = 1280

MOE = [(8, 2, 176, 704), (16, 6, 176, 0)]
MOE_TILES = [-(-(e * f + s) // P) for e, k, f, s in MOE]
MOE_GATES = [e + (1 if s else 0) for e, k, f, s in MOE]
PIECES = 3

ARENA = 33200

STAGES = ("attn0", "ffn0", "attn1", "ffn1")

F32 = mybir.dt.float32
BF16 = mybir.dt.bfloat16
ALU = mybir.AluOpType
ACT = mybir.ActivationFunctionType
AX = mybir.AxisListType


class Signal:

    def __init__(self, sem):
        self.sem, self.n = sem, 0

    def by(self, instruction, k=1):
        self.n += k
        return instruction.then_inc(self.sem, k)


def build(nc, io):
    ctx = ExitStack()
    with ctx:
        def sb(name, shape, dt=F32):
            return ctx.enter_context(nc.sbuf_tensor(name, shape, dt))

        def sem(name):
            return ctx.enter_context(nc.semaphore(name))

        bank = [ctx.enter_context(nc.psum_tensor(f"bank{i}", [P, 512], F32)) for i in range(8)]

        x_sb = sb("x_sb", [P, NT, DIM])
        xn = sb("xn", [P, NT, DIM])
        xnT = sb("xnT", [P, KD, TOK])
        ident = sb("ident", [P, P])
        identb = sb("identb", [P, P], BF16)
        causal_t = sb("causal_t", [P, P])
        headmask = sb("headmask", [P, P])
        chunkmask = sb("chunkmask", [P, P])
        stats = sb("stats", [P, NT, 6])
        mv = sb("mv", [P, NT, 2])
        std = sb("std", [P, NT])
        rstd = sb("rstd", [P, NT])
        eps_ln = sb("eps_ln", [P, 1])
        eps_l2 = sb("eps_l2", [P, 1])

        w_gu = sb("w_gu", [P, 2, 2 * KD * P])
        w_dn = sb("w_dn", [P, 2, DIM])
        rw = [sb(f"rw{s}", [P, KD, MOE_GATES[s]]) for s in range(2)]
        wq_s = sb("wq_s", [P, KD, P])
        wo_s = sb("wo_s", [P, DIM])
        w0 = sb("w0", [P, 5, KD, DIM])
        wo0 = sb("wo0", [P, KD, DIM])
        conv_w = sb("conv_w", [P, 3, KD, CONV])
        norm_w = sb("norm_w", [P, 1])

        arena = sb("arena", [P, ARENA])

        def carve(base, sizes):
            out, at = [], base
            for n in sizes:
                out.append(arena[:, at:at + n])
                at += n
            assert at <= ARENA, at
            return out

        s_const = Signal(sem("s_const"))
        s_x = Signal(sem("s_x"))
        s_out = Signal(sem("s_out"))
        s_xres = Signal(sem("s_xres"))
        n_const = [0]

        consts = [(ident, "ident"), (identb, "identb"), (headmask, "headmask"), (causal_t, "causal_t"),
                  (chunkmask, "chunkmask")]

        class Norm:
            def __init__(self, tag):
                self.st = Signal(sem(f"ln_st_{tag}"))
                self.mv = Signal(sem(f"ln_mv_{tag}"))
                self.std = sem(f"ln_std_{tag}")
                self.rs = Signal(sem(f"ln_rs_{tag}"))
                self.xn = sem(f"ln_xn_{tag}")
                self.tp = sem(f"ln_tp_{tag}")
                self.xT = sem(f"ln_xT_{tag}")

            def dve(self, dve):
                for n in range(NT):
                    self.st.by(nc.vector.bn_stats(stats[:, n, :], x_sb[:, n, :]))
                for n in range(NT):
                    dve.wait_ge(self.st.sem, n + 1)
                    self.mv.by(nc.vector.bn_aggr(mv[:, n, :], stats[:, n, :]))
                dve.wait_ge(self.std, 1)
                self.rs.by(nc.vector.reciprocal(rstd[:], std[:]))
                dve.wait_ge(self.rs.sem, 1)
                for n in range(NT):
                    nc.vector.tensor_scalar(xn[:, n, :], x_sb[:, n, :], mv[:, n, 0:1], rstd[:, n:n + 1],
                                            ALU.subtract, ALU.mult).then_inc(self.xn, 1)

            def act(self, act):
                act.wait_ge(self.mv.sem, NT)
                nc.scalar.activation(std[:], mv[:, :, 1], ACT.Sqrt, bias=eps_ln[:]).then_inc(self.std, 1)
                for q in range(2 * KD):
                    half, k = q // KD, q % KD
                    act.wait_ge(self.tp, q + 1)
                    nc.scalar.copy(xnT[:, k, half * HALF:(half + 1) * HALF], bank[q][:]).then_inc(self.xT, 1)

            def pe(self, pe):
                for q in range(2 * KD):
                    half, k = q // KD, q % KD
                    pe.wait_ge(self.xn, 4 * (half + 1))
                    for j in range(4):
                        mm = nc.tensor.transpose(bank[q][:, j * P:(j + 1) * P],
                                                 xn[:, half * 4 + j, k * P:(k + 1) * P], ident[:])
                    mm.then_inc(self.tp, 1)

        class Moe:
            def __init__(self, s):
                self.s = s
                self.E, self.K, _, _ = MOE[s]
                self.NE = MOE_GATES[s]
                self.tiles = MOE_TILES[s]
                E, NE = self.E, self.NE
                w2 = NT * E * E
                (lg, ex, sm, cw, cr, gt, eq, cws, self.cwT, sg, tt, h) = carve(
                    0, [NT * E, NT * E, 3 * NT, NT * NE, NT * NE, w2, w2, NT * P // 2,
                        TOK // 2, 2 * 512, 2 * 512, 2 * TOK])
                v3 = lambda a, n: a.rearrange("p (t e) -> p t e", e=n)
                self.lg, self.ex, self.cw, self.cr = v3(lg, E), v3(ex, E), v3(cw, NE), v3(cr, NE)
                self.sm = sm.rearrange("p (a t) -> p a t", a=3)
                self.gt = gt.rearrange("p (t i j) -> p t i j", t=NT, i=E)
                self.eq = eq.rearrange("p (t i j) -> p t i j", t=NT, i=E)
                self.gtf, self.eqf = gt, eq
                self.cwsp = cws
                self.cwsr = cws.bitcast(BF16).rearrange("p (t r) -> p t r", t=NT)
                self.cws = self.cwsr[:, :, 0:PIECES * NE].rearrange("p t (a e) -> p t a e", a=PIECES)
                self.selb = sb(f"selb{s}", [P, self.tiles * P], BF16)
                self.cwT = self.cwT.bitcast(BF16)
                self.sg = sg.rearrange("p (r n) -> p r n", r=2)
                self.tt = tt.rearrange("p (r n) -> p r n", r=2)
                self.h = h.rearrange("p (r n) -> p r n", r=2)
                self.tri = sb(f"tri{s}", [P, E * E])
                t = f"{s}"
                self.s_gu = [sem(f"moe_gu_ld{t}_{j}") for j in range(2)]
                self.s_dn = [sem(f"moe_dn_ld{t}_{j}") for j in range(2)]
                self.s_sel0 = sem("moe_sel0" + t)
                self.s_sel = sem("moe_sel" + t)
                self.s_lg = sem("moe_lg" + t)
                self.s_r = Signal(sem("moe_r" + t))
                self.s_sub = sem("moe_sub" + t)
                self.s_exp = Signal(sem("moe_exp" + t))
                self.s_cws = sem("moe_cws" + t)
                self.s_ct = sem("moe_ct" + t)
                self.s_cwT = sem("moe_cwT" + t)
                self.s_pg = sem("moe_pg" + t)
                self.s_pu = sem("moe_pu" + t)
                self.s_pc = sem("moe_pc" + t)
                self.s_silu = sem("moe_silu" + t)
                self.s_mulu = sem("moe_mulu" + t)
                self.s_h = sem("moe_h" + t)
                self.s_pd = sem("moe_pd" + t)

            def loop(self, eng, emit, head=2):
                for i in range(head):
                    emit(i, i % 2, i // 2)
                pairs = (self.tiles - head) // 2
                with eng.Fori(0, pairs) as it:
                    for j in range(2):
                        emit(it * 2 + (head + j), j, it + (head + j) // 2)
                for i in range(head + 2 * pairs, self.tiles):
                    emit(i, i % 2, i // 2)

            def sp(self, sp):
                s = self.s
                sp.wait_ge(self.s_sel0, 1)
                sp.dma_start(self.selb[0:PIECES * self.NE, :], io[f"sel{s}"]).then_inc(self.s_sel, 16)

                def emit(i, j, r):
                    first = isinstance(i, int) and i < 2
                    if not first:
                        sp.wait_ge(self.s_pu, i * 2 - 2)
                    sp.dma_start(w_gu[:, j, :], io[f"w_gu{s}"][bass.ds(i, 1)].rearrange("a p n -> (a p) n")).then_inc(self.s_gu[j], 16)
                    if not first:
                        sp.wait_ge(self.s_pd, i - 1)
                    sp.dma_start(w_dn[:, j, :], io[f"w_dn{s}"][bass.ds(i, 1)].rearrange("a p n -> (a p) n")).then_inc(self.s_dn[j], 16)
                self.loop(sp, emit)

            def pe(self, pe, norm):
                s, E, NE = self.s, self.E, self.NE
                ring = bank[4:8]
                pe.wait_ge(norm.xT, 2 * KD)
                for n in range(NT):
                    for k in range(KD):
                        mm = nc.tensor.matmul(bank[0][:, n * NE:(n + 1) * NE], xnT[:, k, n * P:(n + 1) * P],
                                              rw[s][:, k, :], start=(k == 0), stop=(k == KD - 1))
                mm.then_inc(self.s_lg, 1)

                def down(i, j, r, first=False):
                    pe.wait_ge(self.s_h, i * 2 + 2)
                    pe.wait_ge(self.s_dn[j], r * 16 + 16)
                    for n in range(NT):
                        mm = nc.tensor.matmul(bank[n // 2][:, (n % 2) * DIM:(n % 2 + 1) * DIM],
                                              self.h[:, j, n * P:(n + 1) * P], w_dn[:, j, :],
                                              start=first and n % 2 == 0, stop=True, skip_group_check=True)
                    mm.then_inc(self.s_pd, 1)

                def emit(i, j, r):
                    static = isinstance(i, int)
                    pe.wait_ge(self.s_gu[j], r * 16 + 16)
                    for half in range(2):
                        m = i * 2 + half
                        at = 3 * (2 * j + half)
                        early = static and m < 2
                        rhs = [xnT[:, k, half * HALF:(half + 1) * HALF] for k in range(KD)]
                        if not early:
                            pe.wait_ge(self.s_h, m - 1)
                        for k in range(KD):
                            mm = nc.tensor.matmul(ring[at % 4][:], w_gu[:, j, k * P:(k + 1) * P], rhs[k],
                                                  start=(k == 0), stop=(k == KD - 1))
                        mm.then_inc(self.s_pg, 1)
                        if not (static and m < 1):
                            pe.wait_ge(self.s_silu, m)
                        for k in range(KD):
                            mm = nc.tensor.matmul(ring[(at + 1) % 4][:], w_gu[:, j, (KD + k) * P:(KD + k + 1) * P],
                                                  rhs[k], start=(k == 0), stop=(k == KD - 1))
                        mm.then_inc(self.s_pu, 1)
                        if static and m == 0:
                            pe.wait_ge(self.s_cws, 1)
                            ctb = bank[1][:].bitcast(BF16)
                            for n in range(NT):
                                mm = nc.tensor.transpose(ctb[:, n * P:(n + 1) * P], self.cwsr[:, n, :], identb[:])
                            mm.then_inc(self.s_ct, 1)
                            pe.wait_ge(self.s_cwT, 1)
                            pe.wait_ge(self.s_sel, 16)
                        if not (static and m < 1):
                            pe.wait_ge(self.s_mulu, m)
                        nc.tensor.matmul(ring[(at + 2) % 4][:], self.selb[:, bass.ds(i * P, P)],
                                         self.cwT[:, half * HALF:(half + 1) * HALF],
                                         start=True, stop=True).then_inc(self.s_pc, 1)
                        if half == 0 and not (static and i == 0):
                            down(i - 1, 1 - j, r if j else r - 1, first=static and i == 1)
                self.loop(pe, emit)
                down(self.tiles - 1, (self.tiles - 1) % 2, (self.tiles - 1) // 2)

            def act(self, act):
                E = self.E
                act.wait_ge(self.s_sub, 1)
                self.s_exp.by(nc.scalar.activation(self.ex[:], self.lg[:], ACT.Exp))
                if self.NE > E:
                    self.s_exp.by(nc.scalar.activation(self.sm[:, 2, :], self.psr()[:, :, E], ACT.Exp, scale=-1.0))

                def emit(i, j, r):
                    static = isinstance(i, int)
                    for half in range(2):
                        m = i * 2 + half
                        act.wait_ge(self.s_pg, m + 1)
                        if not (static and m < 2):
                            act.wait_ge(self.s_mulu, m - 1)
                        nc.scalar.activation(self.sg[:, half, :], bank[4 + 3 * (2 * j + half) % 4][:],
                                             ACT.Silu).then_inc(self.s_silu, 1)
                        if static and m == 0:
                            act.wait_ge(self.s_ct, 1)
                            nc.scalar.copy(self.cwT[:], bank[1][:].bitcast(BF16)).then_inc(self.s_cwT, 1)
                self.loop(act, emit)

            def psr(self):
                return bank[0][:, 0:NT * self.NE].rearrange("p (t e) -> p t e", e=self.NE)

            def dve(self, dve):
                E, NE, K = self.E, self.NE, self.K
                psr = self.psr()
                r = self.s_r

                def step(ins):
                    r.by(ins)
                    dve.wait_ge(r.sem, r.n)

                over_e = lambda a: a.unsqueeze(2).to_broadcast([P, NT, E])
                dve.wait_ge(self.s_lg, 1)
                step(nc.vector.memset(self.cwsp, 0.0))
                step(nc.vector.tensor_reduce(self.sm[:, 0, :], psr[:, :, 0:E], AX.X, ALU.max))
                nc.vector.tensor_tensor(self.lg[:], psr[:, :, 0:E], over_e(self.sm[:, 0, :]),
                                        ALU.subtract).then_inc(self.s_sub, 1)
                dve.wait_ge(self.s_exp.sem, 1)
                step(nc.vector.tensor_reduce(self.sm[:, 0, :], self.ex[:], AX.X, ALU.add))
                step(nc.vector.reciprocal(self.sm[:, 1, :], self.sm[:, 0, :]))
                step(nc.vector.tensor_tensor(self.ex[:], self.ex[:], over_e(self.sm[:, 1, :]), ALU.mult))
                p_i = self.ex.unsqueeze(3).to_broadcast([P, NT, E, E])
                p_j = self.ex.unsqueeze(2).to_broadcast([P, NT, E, E])
                step(nc.vector.tensor_tensor(self.gt[:], p_j, p_i, ALU.is_gt))
                step(nc.vector.tensor_tensor(self.eq[:], p_j, p_i, ALU.is_equal))
                eqf = self.eqf.rearrange("p (t n) -> p t n", t=NT)
                step(nc.vector.tensor_tensor(eqf, eqf, self.tri[:].unsqueeze(1).to_broadcast([P, NT, E * E]), ALU.mult))
                step(nc.vector.tensor_tensor(self.gtf, self.gtf, self.eqf, ALU.add))
                step(nc.vector.tensor_reduce(self.lg[:], self.gt[:], AX.X, ALU.add))
                step(nc.vector.scalar_tensor_tensor(out=self.cw[:, :, 0:E], in0=self.lg[:], scalar=float(K),
                                                    in1=self.ex[:], op0=ALU.is_lt, op1=ALU.mult))
                if NE > E:
                    dve.wait_ge(self.s_exp.sem, 2)
                    step(nc.vector.tensor_scalar(self.sm[:, 2, :], self.sm[:, 2, :], 1.0, None, ALU.add))
                    step(nc.vector.reciprocal(self.cw[:, :, E], self.sm[:, 2, :]))
                step(nc.vector.tensor_copy(self.cws[:, :, 0, :], self.cw[:]))
                step(nc.vector.tensor_tensor(self.cr[:], self.cw[:], self.cws[:, :, 0, :], ALU.subtract))
                step(nc.vector.tensor_copy(self.cws[:, :, 1, :], self.cr[:]))
                step(nc.vector.tensor_tensor(self.cr[:], self.cr[:], self.cws[:, :, 1, :], ALU.subtract))
                nc.vector.tensor_copy(self.cws[:, :, 2, :], self.cr[:]).then_inc(self.s_cws, 1)

                def emit(i, j, r):
                    static = isinstance(i, int)
                    for half in range(2):
                        m = i * 2 + half
                        at = 3 * (2 * j + half)
                        dve.wait_ge(self.s_silu, m + 1)
                        dve.wait_ge(self.s_pu, m + 1)
                        nc.vector.tensor_tensor(self.tt[:, half, :], self.sg[:, half, :],
                                                bank[4 + (at + 1) % 4][:], ALU.mult).then_inc(self.s_mulu, 1)
                        dve.wait_ge(self.s_mulu, m + 1)
                        dve.wait_ge(self.s_pc, m + 1)
                        if not (static and i < 2):
                            dve.wait_ge(self.s_pd, i - 1)
                        nc.vector.tensor_tensor(self.h[:, j, half * HALF:(half + 1) * HALF], self.tt[:, half, :],
                                                bank[4 + (at + 2) % 4][:], ALU.mult).then_inc(self.s_h, 1)
                self.loop(dve, emit)
                dve.wait_ge(self.s_pd, self.tiles)
                add_residual(dve)

        def add_residual(dve):
            for q in range(4):
                v = x_sb[:, 2 * q:2 * q + 2, :].rearrange("p t c -> p (t c)")
                s_xres.by(nc.vector.tensor_tensor(v, v, bank[q][:], ALU.add))
            dve.wait_ge(s_xres.sem, s_xres.n)

        stages = []
        for tag in STAGES:
            norm = Norm(tag)
            if tag.startswith("ffn"):
                stages.append((norm, Moe(int(tag[-1]))))
            elif tag == "attn1":
                stages.append((norm, make_attn1(nc, io, sem, sb, carve, bank, dict(
                    xnT=xnT, ident=ident, wq_s=wq_s, wo_s=wo_s, x_sb=x_sb, causal_t=causal_t, s_xres=s_xres))))
            else:
                stages.append((norm, make_attn0(nc, io, sem, sb, carve, bank, dict(
                    xnT=xnT, ident=ident, headmask=headmask, chunkmask=chunkmask, w0=w0, wo0=wo0, conv_w=conv_w,
                    norm_w=norm_w, eps_l2=eps_l2, eps_ln=eps_ln, x_sb=x_sb, s_xres=s_xres, add_residual=add_residual))))
        for norm, st in stages:
            if isinstance(st, Moe):
                consts.append((st.tri, f"tri{st.s}"))
                consts.append((rw[st.s], f"rw{st.s}"))
        if "attn0" in STAGES:
            consts += [(w0, "w0"), (wo0, "wo0"), (conv_w, "conv_w"), (norm_w, "norm_w")]
        n_load = 16 * len(consts)
        s_eps = sem("s_eps")

        block = ctx.enter_context(nc.Block())

        @block.sync
        def _(sp):
            sp.dma_start(x_sb[:], io["x"]).then_inc(s_x.sem, 16)
            for dst, name in consts:
                sp.dma_start(dst[:], io[name]).then_inc(s_const.sem, 16)
            for norm, st in stages:
                st.sp(sp)
            sp.wait_ge(s_xres.sem, 4 * len(stages))
            sp.dma_start(io["out"], x_sb[:]).then_inc(s_out.sem, 16)
            sp.wait_ge(s_out.sem, 16)

        @block.gpsimd
        def _(pool):
            pool.memset(eps_ln[:], EPS).then_inc(s_eps, 1)
            pool.memset(eps_l2[:], L2_EPS).then_inc(s_eps, 1)
            for norm, st in stages:
                if isinstance(st, Moe):
                    pool.memset(st.selb[:], 0.0).then_inc(st.s_sel0, 1)
            pool.wait_ge(s_const.sem, n_load)
            for norm, st in stages:
                if hasattr(st, "pool"):
                    st.pool(pool, norm)

        @block.scalar
        def _(act):
            act.wait_ge(s_eps, 2)
            act.wait_ge(s_const.sem, n_load)
            for norm, st in stages:
                norm.act(act)
                st.act(act)

        @block.tensor
        def _(pe):
            pe.wait_ge(s_const.sem, n_load)
            for norm, st in stages:
                norm.pe(pe)
                st.pe(pe, norm)

        @block.vector
        def _(dve):
            dve.wait_ge(s_x.sem, 16)
            dve.wait_ge(s_const.sem, n_load)
            for norm, st in stages:
                norm.dve(dve)
                st.dve(dve)


def make_attn1(nc, io, sem, sb, carve, bank, g):
    xnT, ident, wq_s, wo_s, x_sb = g["xnT"], g["ident"], g["wq_s"], g["wo_s"], g["x_sb"]
    causal_t = g["causal_t"]
    s_xres, xres_base = g["s_xres"], 4 * STAGES.index("attn1")
    NGRP = BATCH * HKV
    NH = BATCH * HQ
    (kT, v, th, pr, qr, rt, ru, on, oT) = carve(
        0, [NGRP * SEQ, NGRP * KT * (DH + 1), P_ALL, P_ALL, SEQ, SEQ, SEQ, SEQ, SEQ])
    kT = kT.rearrange("p (g t) -> p g t", g=NGRP)
    v = v.rearrange("p (g k d) -> p g k d", g=NGRP, k=KT)
    cosT, sinT = sb("cosT", [P, SEQ]), sb("sinT", [P, SEQ])
    wkv = sb("wkv", [P, HKV, 2, KD, DH])
    rc = sb("rc", [P, KT])
    b_q, b_s, b_o, b_y = bank[0], bank[1:4], bank[4:6], bank[6:8]

    s_cs = sem("a1_cs")
    s_wq = sem("a1_wq")
    s_wo = sem("a1_wo")
    s_one = sem("a1_one")
    s_k = sem("a1_k")
    s_v = sem("a1_v")
    s_ve = sem("a1_ve")
    s_q = sem("a1_q")
    s_rot = sem("a1_rot")
    s_qr = sem("a1_qr")
    s_sc = sem("a1_sc")
    s_th = sem("a1_th")
    s_ex = sem("a1_ex")
    s_p = sem("a1_p")
    s_pv = sem("a1_pv")
    s_rc = sem("a1_rc")
    s_on = sem("a1_on")
    s_tp = sem("a1_tp")
    s_oT = sem("a1_oT")
    s_y = sem("a1_y")

    class Attn1:
        def heads(self, eng, emit):
            for grp in range(NGRP):
                for j in range(2):
                    emit(grp * REP + j, grp)
                with eng.Fori(0, REP - 3) as it:
                    emit(it + (grp * REP + 2), grp)
                emit(grp * REP + REP - 1, grp)

        def sp(self, sp):
            sp.dma_start(cosT[:], io["cosT"]).then_inc(s_cs, 16)
            sp.dma_start(sinT[:], io["sinT"]).then_inc(s_cs, 16)
            sp.dma_start(wkv[:], io["wkv"]).then_inc(s_cs, 16)

            def load_q(h):
                sp.dma_start(wq_s[:], io["wq1"][bass.ds(h, 1)].rearrange("a p k n -> (a p) k n")).then_inc(s_wq, 16)

            def load_o(h):
                sp.dma_start(wo_s[:], io["wo1"][bass.ds(h, 1)].rearrange("a p n -> (a p) n")).then_inc(s_wo, 16)

            load_q(0)
            load_o(0)

            def emit(n, grp):
                h = n - HQ * (grp // HKV)
                static = isinstance(n, int)
                if not (static and n == NH - 1):
                    sp.wait_ge(s_q, n + 1)
                    load_q((n + 1) % HQ if static else h + 1)
                if not (static and n == 0):
                    sp.wait_ge(s_y, n)
                    load_o(h)
            self.heads(sp, emit)

        def pool(self, pool, norm):
            pool.wait_ge(norm.xT, 2 * KD)
            pool.memset(v[:, :, :, DH:DH + 1], 1.0).then_inc(s_one, 1)

            def emit(n, grp):
                pool.wait_ge(s_ex, n + 1)
                for at, gap in ((0, 512), (P_OFF[3], P)):
                    blocks = pr[:, at:at + 2 * gap].rearrange("p (a n) -> p a n", a=2)[:, :, 0:P]
                    nc.gpsimd.tensor_tensor(blocks, blocks, causal_t[:].unsqueeze(1).to_broadcast([P, 2, P]),
                                            ALU.mult).then_inc(s_p, 1)
            self.heads(pool, emit)

        def act(self, act):
            for grp in range(NGRP):
                act.wait_ge(s_v, grp + 1)
                nc.scalar.copy(v[:, grp, :, 0:DH], b_s[grp % 2][:].rearrange("p (k d) -> p k d", k=KT))\
                   .then_inc(s_ve, 1)

            def emit(n, grp):
                if not (isinstance(n, int) and n == 0):
                    act.wait_ge(s_ex, n)
                for sbank, w in enumerate((512, 512, 256)):
                    act.wait_ge(s_sc, n * 3 + 1 + sbank)
                    nc.scalar.activation(th[:, sbank * 512:sbank * 512 + w], b_s[sbank][:, 0:w], ACT.Tanh,
                                         scale=SCALE / SOFTCAP).then_inc(s_th, 1)
                act.wait_ge(s_th, n * 3 + 3)
                if not (isinstance(n, int) and n == 0):
                    act.wait_ge(s_pv, n * 2)
                nc.scalar.activation(pr[:], th[:], ACT.Exp, scale=SOFTCAP).then_inc(s_ex, 1)
            self.heads(act, emit)

        def pe(self, pe, norm):
            pe.wait_ge(s_cs, 48)
            pe.wait_ge(norm.xT, 2 * KD)
            for grp in range(NGRP):
                b, kv = grp // HKV, grp % HKV
                if grp:
                    pe.wait_ge(s_rot, 3 * grp)
                for k in range(KD):
                    mm = nc.tensor.matmul(b_q[:], wkv[:, kv, 0, k, :], xnT[:, k, b * SEQ:(b + 1) * SEQ],
                                          start=(k == 0), stop=(k == KD - 1))
                mm.then_inc(s_k, 1)
                if grp >= 2:
                    pe.wait_ge(s_ve, grp - 1)
                for kt in range(KT):
                    for k in range(KD):
                        at = b * SEQ + kt * P
                        mm = nc.tensor.matmul(b_s[grp % 2][:, kt * DH:(kt + 1) * DH], xnT[:, k, at:at + P],
                                              wkv[:, kv, 1, k, :], start=(k == 0), stop=(k == KD - 1))
                mm.then_inc(s_v, 1)

            def queries(n, b):
                pe.wait_ge(s_rot, (n + NGRP) * 3)
                pe.wait_ge(s_wq, n * 16 + 16)
                for k in range(KD):
                    mm = nc.tensor.matmul(b_q[:], wq_s[:, k, :], xnT[:, k, b * SEQ:(b + 1) * SEQ],
                                          start=(k == 0), stop=(k == KD - 1))
                mm.then_inc(s_q, 1)

            def project(n):
                first = isinstance(n, int) and n % HQ == 0
                pe.wait_ge(s_oT, n * 2 + 2)
                pe.wait_ge(s_wo, n * 16 + 16)
                if first and n:
                    pe.wait_ge(s_xres.sem, xres_base + 2)
                for t in range(KT):
                    mm = nc.tensor.matmul(b_y[t // 2][:, (t % 2) * DIM:(t % 2 + 1) * DIM],
                                          oT[:, t * P:(t + 1) * P], wo_s[:],
                                          start=first and t % 2 == 0, stop=True, skip_group_check=True)
                mm.then_inc(s_y, 1)

            def turn(n):
                for pair in range(2):
                    pe.wait_ge(s_on, n * 2 + 1 + pair)
                    for t in range(2):
                        at = (pair * 2 + t) * P
                        mm = nc.tensor.transpose(b_o[pair][:, t * P:(t + 1) * P], on[:, at:at + P], ident[:])
                    mm.then_inc(s_tp, 1)

            queries(0, 0)
            pe.wait_ge(s_ve, NGRP)
            pe.wait_ge(s_one, 1)

            def emit(n, grp):
                static = isinstance(n, int)
                pe.wait_ge(s_qr, n + (1 + NGRP))
                for sbank, kts in enumerate([[0], [1, 3], [2]]):
                    if not (static and n == 0):
                        pe.wait_ge(s_th, n * 3 - 2 + sbank)
                    for kt in kts:
                        w = SEQ - kt * P
                        at = P_OFF[kt] - 512 * sbank
                        mm = nc.tensor.matmul(b_s[sbank][:, at:at + w], kT[:, grp, kt * P:(kt + 1) * P],
                                              qr[:, kt * P:SEQ], start=True, stop=True, skip_group_check=True)
                    mm.then_inc(s_sc, 1)
                if not (static and n == 0):
                    turn(n - 1)
                if not (static and n == NH - 1):
                    queries(n + 1, (n + 1) // HQ if static else grp // HKV)
                if not (static and n == 0):
                    project(n - 1)
                pe.wait_ge(s_p, n * 2 + 2)
                for pair in range(2):
                    for t in range(2):
                        qb = pair * 2 + t
                        for kt in range(qb + 1):
                            at = P_OFF[kt] + (qb - kt) * P
                            mm = nc.tensor.matmul(b_o[pair][:, t * (DH + 1):(t + 1) * (DH + 1)],
                                                  pr[:, at:at + P], v[:, grp, kt, :],
                                                  start=(kt == 0), stop=(kt == qb))
                    mm.then_inc(s_pv, 1)
            self.heads(pe, emit)
            turn(NH - 1)
            project(NH - 1)

        def dve(self, dve):
            def rotate(r, dst):
                hd = DH // 2
                if not (isinstance(r, int) and r == 0):
                    dve.wait_ge(s_qr, r)
                nc.vector.tensor_tensor(rt[0:hd, :], b_q[hd:P, :], sinT[hd:P, :], ALU.mult).then_inc(s_rot, 1)
                nc.vector.tensor_tensor(rt[hd:P, :], b_q[0:hd, :], sinT[0:hd, :], ALU.mult).then_inc(s_rot, 1)
                nc.vector.tensor_tensor(ru[:], b_q[:], cosT[:], ALU.mult).then_inc(s_rot, 1)
                dve.wait_ge(s_rot, r * 3 + 3)
                nc.vector.tensor_tensor(dst, rt[:], ru[:], ALU.add).then_inc(s_qr, 1)

            dve.wait_ge(s_cs, 48)
            for grp in range(NGRP):
                dve.wait_ge(s_k, grp + 1)
                rotate(grp, kT[:, grp, :])

            def turned(n, static):
                if not (static and n == 0):
                    dve.wait_ge(s_y, n)
                for pair in range(2):
                    dve.wait_ge(s_tp, n * 2 + 1 + pair)
                    nc.vector.tensor_copy(oT[:, pair * 2 * P:(pair + 1) * 2 * P],
                                          b_o[pair][:, 0:2 * P]).then_inc(s_oT, 1)

            def residual(b):
                dve.wait_ge(s_y, HQ * (b + 1))
                for q in range(2):
                    t = b * KT + 2 * q
                    xv = x_sb[:, t:t + 2, :].rearrange("p t c -> p (t c)")
                    s_xres.by(nc.vector.tensor_tensor(xv, xv, b_y[q][:], ALU.add))

            dve.wait_ge(s_q, 1)
            rotate(NGRP, qr[:])

            def emit(n, grp):
                static = isinstance(n, int)
                if not (static and n == 0):
                    turned(n - 1, static)
                if not (static and n == NH - 1):
                    dve.wait_ge(s_q, n + 2)
                    dve.wait_ge(s_sc, n * 3 + 3)
                    rotate(n + (1 + NGRP), qr[:])
                if static and n == HQ:
                    residual(0)
                for pair in range(2):
                    dve.wait_ge(s_pv, n * 2 + 1 + pair)
                    o = b_o[pair][:, 0:2 * (DH + 1)].rearrange("p (t d) -> p t d", t=2)
                    nc.vector.reciprocal(rc[:, 2 * pair:2 * pair + 2], o[:, :, DH]).then_inc(s_rc, 1)
                    dve.wait_ge(s_rc, n * 2 + 1 + pair)
                    nc.vector.tensor_tensor(on[:, pair * 2 * P:(pair + 1) * 2 * P].rearrange("p (t d) -> p t d", t=2),
                                            o[:, :, 0:DH],
                                            rc[:, 2 * pair:2 * pair + 2].unsqueeze(2).to_broadcast([P, 2, DH]),
                                            ALU.mult).then_inc(s_on, 1)
            self.heads(dve, emit)
            turned(NH - 1, True)
            residual(1)
            dve.wait_ge(s_xres.sem, s_xres.n)

    return Attn1()


def make_attn0(nc, io, sem, sb, carve, bank, g):
    xnT, ident, headmask, chunkmask = g["xnT"], g["ident"], g["headmask"], g["chunkmask"]
    w0, wo0, conv_w, norm_w, eps_l2, eps_ln = (g[n] for n in ("w0", "wo0", "conv_w", "norm_w", "eps_l2", "eps_ln"))
    x_sb, s_xres = g["x_sb"], g["s_xres"]
    N = NU * CH
    PADW = SEQ + CONV - 1
    NP = 2 * BATCH * PADW
    K_, Q_, V_, B_, G_ = range(5)
    bufs = carve(0, [NP] * 3 + [N] * 10 + [NG * P] * 12)
    pad = [b.rearrange("p (a b t) -> p a b t", a=2, b=BATCH) for b in bufs[0:3]]
    kd, bkd, vd = (b[:, 0:N] for b in bufs[0:3])
    kc, qc, vc, betac, gatec, bkc, r1, r2, pr, op = bufs[3:13]
    kp, vp, tt = vc, betac, bkd
    xc = [kc, qc, vc]
    sq = [pr, op]
    rn = [r1, r2]
    am, tm = r1, r2
    od, oc = kd, tm
    ex = [[bufs[13 + 2 * n + r].rearrange("p (g n) -> p g n", g=NG) for r in range(2)] for n in range(6)]
    KX, QX, BKX, TX, KKX, PX = range(6)
    st = sb("state", [P, 2, NG, D0])
    rr = sb("rr", [P, NG, D0])
    uu = sb("uu", [P, NG, D0])
    ss = sb("ss", [P, NU])
    sr = sb("sr", [P, NU])

    s_pp = sem("a0_pp")
    s_pe = sem("a0_pe")
    s_pz = sem("a0_pz")
    s_cv = sem("a0_cv")
    s_si = sem("a0_si")
    s_sq = sem("a0_sq")
    s_ns = sem("a0_ns")
    s_nr = sem("a0_nr")
    s_kq = Signal(sem("a0_kq"))
    s_bk = sem("a0_bk")
    s_td = sem("a0_td")
    s_te = sem("a0_te")
    s_am = Signal(sem("a0_am"))
    s_tk = sem("a0_tk")
    s_tke = sem("a0_tke")
    s_ex = sem("a0_ex")
    s_exp = sem("a0_exp")
    s_pm = sem("a0_pm")
    s_px = sem("a0_px")
    s_R = sem("a0_R")
    s_Rv = sem("a0_Rv")
    s_U = sem("a0_U")
    s_Uv = sem("a0_Uv")
    s_KU = sem("a0_KU")
    s_S = sem("a0_S")
    s_O = sem("a0_O")
    s_Ov = sem("a0_Ov")
    s_rm = Signal(sem("a0_rm"))
    s_rs = sem("a0_rs")
    s_to = sem("a0_to")
    s_toe = sem("a0_toe")
    s_tc = sem("a0_tc")
    s_tce = sem("a0_tce")
    s_y = sem("a0_y")

    def by_token(a):
        return a.rearrange("p (u i) -> p i u", i=CH)

    def chunk(a, c):
        return a.rearrange("p (g c i) -> p g c i", g=NG, i=CH)[:, :, bass.ds(c, 1), :].rearrange("p g a i -> p g (a i)")

    def chunk_last(a, c):
        return a.rearrange("p (x g c) -> p g x c", x=CH, g=NG)[:, :, :, bass.ds(c, 1)].rearrange("p g x a -> p g (x a)")

    hm = headmask[:].rearrange("p (h x) -> p h x", x=D0)[:, :, 0]

    def spread(e, dst, src):
        return e.tensor_tensor(dst[:].rearrange("p g (h x) -> p g h x", h=HH),
                               src.unsqueeze(2).to_broadcast([P, NG, HH, D0]),
                               hm.unsqueeze(1).unsqueeze(3).to_broadcast([P, NG, HH, D0]), ALU.mult)

    class Attn0:
        def chunks(self, eng, emit):
            for c in range(2):
                emit(c, c)
            with eng.Fori(0, (NCH - 4) // 2) as it:
                for r in range(2):
                    emit(it * 2 + (2 + r), r)
            for c in range(NCH - 2, NCH):
                emit(c, c % 2)

        def sp(self, sp):
            pass

        def pe(self, pe, norm):
            pe.wait_ge(norm.xT, 2 * KD)
            q = 0
            for t in range(5):
                for a in range(2):
                    for b in range(BATCH):
                        if q >= 4:
                            pe.wait_ge(s_pe, q - 3)
                        for k in range(KD):
                            mm = nc.tensor.matmul(bank[4 + q % 4][:], w0[:, t, k, a * P:(a + 1) * P],
                                                  xnT[:, k, b * SEQ:(b + 1) * SEQ], start=(k == 0), stop=(k == KD - 1))
                        mm.then_inc(s_pp, 1)
                        q += 1
            pe.wait_ge(s_pe, 20)
            for t in range(2):
                pe.wait_ge(s_sq, t + 1)
                for j in range(4):
                    nc.tensor.matmul(bank[t * 4 + j][:], headmask[:], sq[t][:, j * 512:(j + 1) * 512],
                                     start=True, stop=True).then_inc(s_ns, 1)
            nt = 0
            for t, src in enumerate((kc, bkc, vc)):
                if t == 0:
                    pe.wait_ge(s_kq.sem, 2)
                else:
                    pe.wait_ge(s_bk, t)
                for j in range(4):
                    if t == 0:
                        pe.wait_ge(s_nr, j + 1)
                    elif t == 1:
                        pe.wait_ge(s_nr, 4 + j + 1)
                    else:
                        pe.wait_ge(s_te, nt - 7)
                    for i in range(4):
                        mm = nc.tensor.transpose(bank[nt % 8][:, i * P:(i + 1) * P], by_token(src)[:, 4 * j + i, :],
                                                 ident[:])
                    mm.then_inc(s_td, 1)
                    nt += 1
            nk = 0
            for t, src in enumerate((kd, vd, tm)):
                pe.wait_ge(s_te, (4, 12, 12)[t])
                if t == 2:
                    pe.wait_ge(s_am.sem, self.n_am)
                for j in range(4):
                    if nk >= 4:
                        pe.wait_ge(s_tke, nk - 3)
                    elif nk == 0:
                        pe.wait_ge(s_te, 12)
                    for i in range(4):
                        x = 4 * j + i
                        col = src.rearrange("p (c x) -> p x c", x=D0)[:, x, :]
                        mm = nc.tensor.transpose(bank[nk % 4][:, i * P:(i + 1) * P], col, ident[:])
                    mm.then_inc(s_tk, 1)
                    nk += 1

            def pmat(c, r):
                pe.wait_ge(s_ex, c * 3 + 2)
                if not (isinstance(c, int) and c == 0):
                    pe.wait_ge(s_px, c)
                for gr in range(NG):
                    mm = nc.tensor.matmul(bank[4][:, gr * P:(gr + 1) * P], ex[KX][r][:, gr, :], ex[QX][r][:, gr, :],
                                          start=True, stop=True, skip_group_check=True)
                mm.then_inc(s_pm, 1)

            def group(b, gr):
                return bank[b][:, gr * D0:(gr + 1) * D0]

            pe.wait_ge(s_tke, 12)
            pmat(0, 0)

            def emit(c, r):
                static = isinstance(c, int)
                pe.wait_ge(s_ex, c * 3 + 3)
                pe.wait_ge(s_S, c + 1)
                for gr in range(NG):
                    mm = nc.tensor.matmul(group(5, gr), ex[BKX][r][:, gr, :], st[:, r, gr, :], start=True, stop=True,
                                          skip_group_check=True)
                mm.then_inc(s_R, 1)
                if not (static and c < 2):
                    pe.wait_ge(s_Ov, c - 1)
                for gr in range(NG):
                    nc.tensor.matmul(group(r, gr), ex[QX][r][:, gr, :], st[:, r, gr, :], start=(gr == 0), stop=False,
                                     skip_group_check=True)
                pe.wait_ge(s_exp, c * 2 + 2)
                pe.wait_ge(s_Rv, c + 1)
                for gr in range(NG):
                    mm = nc.tensor.matmul(group(6, gr), ex[TX][r][:, gr, :], rr[:, gr, :], start=True, stop=True,
                                          skip_group_check=True)
                mm.then_inc(s_U, 1)
                if not (static and c == NCH - 1):
                    pmat(c + 1, 1 - r)
                pe.wait_ge(s_Uv, c + 1)
                for gr in range(NG):
                    mm = nc.tensor.matmul(group(7, gr), ex[KKX][r][:, gr, :], uu[:, gr, :], start=True, stop=True,
                                          skip_group_check=True)
                mm.then_inc(s_KU, 1)
                pe.wait_ge(s_px, c + 1)
                for gr in range(NG):
                    mm = nc.tensor.matmul(group(r, gr), ex[PX][r][:, gr, :], uu[:, gr, :], start=False, stop=True,
                                          skip_group_check=True)
                mm.then_inc(s_O, 1)
            self.chunks(pe, emit)

            pe.wait_ge(s_rm.sem, self.n_rm)
            for j in range(4):
                for i in range(4):
                    x = 4 * j + i
                    mm = nc.tensor.transpose(bank[j][:, i * P:(i + 1) * P], op[:, x * NU:(x + 1) * NU], ident[:])
                mm.then_inc(s_to, 1)
            pe.wait_ge(s_toe, 4)
            for j in range(4):
                for i in range(4):
                    mm = nc.tensor.transpose(bank[4 + j][:, i * P:(i + 1) * P],
                                             od.rearrange("p (c i) -> p i c", i=CH)[:, 4 * j + i, :], ident[:])
                mm.then_inc(s_tc, 1)
            pe.wait_ge(s_tce, 4)
            for n in range(NT):
                for k in range(KD):
                    mm = nc.tensor.matmul(bank[n // 2][:, (n % 2) * DIM:(n % 2 + 1) * DIM],
                                          oc[:, k * TOK + n * P:k * TOK + (n + 1) * P], wo0[:, k, :],
                                          start=(k == 0), stop=(k == KD - 1), skip_group_check=True)
            mm.then_inc(s_y, 1)

        def act(self, act):
            act.wait_ge(s_pz, 3)
            q = 0
            for t in range(5):
                for a in range(2):
                    for b in range(BATCH):
                        act.wait_ge(s_pp, q + 1)
                        if t < 3:
                            ins = nc.scalar.copy(pad[t][:, a, b, CONV - 1:PADW], bank[4 + q % 4][:])
                        else:
                            at = a * TOK + b * SEQ
                            ins = nc.scalar.activation((betac if t == B_ else gatec)[:, at:at + SEQ],
                                                       bank[4 + q % 4][:], ACT.Sigmoid)
                        ins.then_inc(s_pe, 1)
                        q += 1
            for t in range(3):
                act.wait_ge(s_cv, 8 * (t + 1))
                nc.scalar.activation(xc[t], xc[t], ACT.Silu).then_inc(s_si, 1)
            for t in range(2):
                act.wait_ge(s_si, t + 1)
                nc.scalar.activation(sq[t], xc[t], ACT.Square).then_inc(s_sq, 1)
            for t in range(2):
                for j in range(4):
                    act.wait_ge(s_ns, 4 * t + j + 1)
                    nc.scalar.activation(rn[t][:, j * 512:(j + 1) * 512], bank[4 * t + j][:], ACT.Sqrt,
                                         bias=eps_l2[:]).then_inc(s_nr, 1)
            for nt in range(12):
                act.wait_ge(s_td, nt + 1)
                dst = (kd, bkd, vd)[nt // 4].rearrange("p (h i d) -> p i h d", h=HH, i=CH)
                j = nt % 4
                nc.scalar.copy(dst[:, 4 * j:4 * j + 4, :, :],
                               bank[nt % 8][:].rearrange("p (i h d) -> p i h d", i=4, h=HH)).then_inc(s_te, 1)
            for nk in range(12):
                act.wait_ge(s_tk, nk + 1)
                nc.scalar.copy((kp, vp, tt)[nk // 4][:, (nk % 4) * 512:(nk % 4 + 1) * 512], bank[nk % 4][:])\
                   .then_inc(s_tke, 1)

            def emit(c, r):
                static = isinstance(c, int)
                act.wait_ge(s_U, c + 1)
                if not (static and c == 0):
                    act.wait_ge(s_O, c)
                nc.scalar.copy(uu[:].rearrange("p g d -> p (g d)"), bank[6][:, 0:NG * D0]).then_inc(s_Uv, 1)
                act.wait_ge(s_O, c + 1)
                nc.scalar.copy(chunk_last(op, c), bank[r][:, 0:NG * D0].rearrange("p (g d) -> p g d", g=NG))\
                   .then_inc(s_Ov, 1)
            self.chunks(act, emit)
            act.wait_ge(s_Ov, NCH)
            nc.scalar.activation(pr, op, ACT.Square).then_inc(s_rs, 1)
            act.wait_ge(s_rm.sem, 1)
            nc.scalar.activation(sr[:], ss[:], ACT.Sqrt, scale=1.0 / D0, bias=eps_ln[:]).then_inc(s_rs, 1)
            for j in range(4):
                act.wait_ge(s_to, j + 1)
                dst = od.rearrange("p (h v i) -> p v h i", h=HH, v=D0)[:, 4 * j:4 * j + 4, :, :]
                nc.scalar.copy(dst, bank[j][:].rearrange("p (v h i) -> p v h i", v=4, h=HH)).then_inc(s_toe, 1)

        def pool(self, pool, norm):
            for t in range(3):
                pool.memset(pad[t][:, :, :, 0:CONV - 1], 0.0).then_inc(s_pz, 1)
            pool.memset(st[:], 0.0).then_inc(s_pz, 1)
            pool.wait_ge(s_pe, 16)
            pool.wait_ge(s_kq.sem, 2)
            nc.gpsimd.tensor_tensor(bkc, kc, betac, ALU.mult).then_inc(s_bk, 1)
            pool.wait_ge(s_si, 3)
            nc.gpsimd.tensor_tensor(vc, vc, betac, ALU.mult).then_inc(s_bk, 1)
            pool.wait_ge(s_tke, 12)

            def emit(c, r):
                if not (isinstance(c, int) and c < 2):
                    pool.wait_ge(s_O, c - 1)
                spread(nc.gpsimd, ex[TX][r], chunk_last(tt, c)).then_inc(s_exp, 1)
                spread(nc.gpsimd, ex[KKX][r], chunk_last(kp, c)).then_inc(s_exp, 1)
            self.chunks(pool, emit)

        def dve(self, dve):
            n = 0
            dve.wait_ge(s_pz, 4)
            for t in range(3):
                dve.wait_ge(s_pe, 4 * (t + 1))
                for tap in range(CONV):
                    for a in range(2):
                        src = pad[t][:, a, :, tap:tap + SEQ]
                        dst = xc[t][:, a * TOK:(a + 1) * TOK].rearrange("p (b t) -> p b t", b=BATCH)
                        w = conv_w[:, t, a, tap:tap + 1]
                        if tap == 0:
                            ins = nc.vector.tensor_scalar(dst, src, w, None, ALU.mult)
                        else:
                            dve.wait_ge(s_cv, n - 1)
                            ins = nc.vector.scalar_tensor_tensor(out=dst, in0=src, scalar=w, in1=dst,
                                                                 op0=ALU.mult, op1=ALU.add)
                        ins.then_inc(s_cv, 1)
                        n += 1
            for t in range(2):
                dve.wait_ge(s_nr, 4 * (t + 1))
                s_kq.by(nc.vector.reciprocal(rn[t], rn[t]))
                dve.wait_ge(s_kq.sem, s_kq.n)
                if t == 0:
                    s_kq.by(nc.vector.tensor_tensor(kc, kc, rn[t], ALU.mult))
                else:
                    s_kq.by(nc.vector.scalar_tensor_tensor(out=qc, in0=qc, scalar=float(D0) ** -0.5, in1=rn[t],
                                                           op0=ALU.mult, op1=ALU.mult))
            dve.wait_ge(s_kq.sem, 4)

            def step(ins):
                s_am.by(ins)
                dve.wait_ge(s_am.sem, s_am.n)

            step(nc.vector.memset(tm, 0.0))
            step(nc.vector.memset(tm.rearrange("p (h x) -> p h x", h=HH)[:, :, 0:CH * CH:CH + 1], 1.0))
            dve.wait_ge(s_te, 8)
            a4 = am.rearrange("p (h i j) -> p h i j", h=HH, i=CH)
            t4 = tm.rearrange("p (h j i) -> p h i j", h=HH, j=CH)
            k4 = kd.rearrange("p (h i d) -> p h i d", i=CH, h=HH)
            b4 = bkd.rearrange("p (h i d) -> p h i d", i=CH, h=HH)
            for i in range(1, CH):
                prod = pr[:, 0:HH * i * D0].rearrange("p (h j d) -> p h j d", h=HH, j=i)
                step(nc.vector.tensor_tensor(prod, b4[:, :, i, :].unsqueeze(2).to_broadcast([P, HH, i, D0]),
                                             k4[:, :, 0:i, :], ALU.mult))
                step(nc.vector.tensor_reduce(a4[:, :, i, 0:i], prod, AX.X, ALU.add))
            for i in range(1, CH):
                prod = pr[:, 0:HH * i * i].rearrange("p (h x j) -> p h x j", h=HH, x=i)
                step(nc.vector.tensor_tensor(prod, a4[:, :, i, 0:i].unsqueeze(2).to_broadcast([P, HH, i, i]),
                                             t4[:, :, 0:i, 0:i].rearrange("p h j x -> p h x j"), ALU.mult))
                step(nc.vector.tensor_reduce(t4[:, :, i, 0:i], prod, AX.X, ALU.add, negate=True))

            def spread3(c, r):
                for e, src in ((KX, kc), (QX, qc), (BKX, bkc)):
                    spread(nc.vector, ex[e][r], chunk(src, c)).then_inc(s_ex, 1)

            def mask_p(c, r):
                dve.wait_ge(s_pm, c + 1)
                nc.vector.tensor_tensor(ex[PX][r][:], bank[4][:].rearrange("p (g n) -> p g n", g=NG),
                                        chunkmask[:].unsqueeze(1).to_broadcast([P, NG, P]), ALU.mult)\
                  .then_inc(s_px, 1)

            dve.wait_ge(s_bk, 2)
            nc.vector.memset(st[:, 0, :, :], 0.0).then_inc(s_S, 1)
            spread3(0, 0)
            mask_p(0, 0)
            dve.wait_ge(s_tke, 12)

            def emit(c, r):
                static = isinstance(c, int)
                dve.wait_ge(s_R, c + 1)
                nc.vector.tensor_tensor(rr[:], chunk_last(vp, c), bank[5][:, 0:NG * D0].rearrange("p (g d) -> p g d", g=NG),
                                        ALU.subtract).then_inc(s_Rv, 1)
                if not (static and c == 0):
                    dve.wait_ge(s_O, c)
                last = static and c == NCH - 1
                if not last:
                    for e, src in ((KX, kc), (QX, qc), (BKX, bkc)):
                        spread(nc.vector, ex[e][1 - r], chunk(src, c + 1)).then_inc(s_ex, 1)
                dve.wait_ge(s_KU, c + 1)
                nc.vector.tensor_tensor(st[:, 1 - r, :, :], st[:, r, :, :],
                                        bank[7][:, 0:NG * D0].rearrange("p (g d) -> p g d", g=NG),
                                        ALU.add).then_inc(s_S, 1)
                if not last:
                    mask_p(c + 1, 1 - r)
            self.chunks(dve, emit)
            ov = op.rearrange("p (v u) -> p u v", v=D0)
            dve.wait_ge(s_rs, 1)
            s_rm.by(nc.vector.tensor_reduce(ss[:], pr.rearrange("p (v u) -> p u v", v=D0), AX.X, ALU.add))
            dve.wait_ge(s_rs, 2)
            s_rm.by(nc.vector.reciprocal(ss[:], sr[:]))
            dve.wait_ge(s_rm.sem, 2)
            s_rm.by(nc.vector.tensor_tensor(op.rearrange("p (v u) -> p v u", v=D0), op.rearrange("p (v u) -> p v u", v=D0),
                                            ss[:].unsqueeze(1).to_broadcast([P, D0, NU]), ALU.mult))
            for j in range(4):
                dve.wait_ge(s_tc, j + 1)
                tok = lambda a: a.rearrange("p (u i) -> p i u", i=CH)[:, 4 * j:4 * j + 4, :]
                nc.vector.scalar_tensor_tensor(out=tok(oc), in0=bank[4 + j][:].rearrange("p (i u) -> p i u", i=4),
                                               scalar=norm_w[:, 0:1], in1=tok(gatec), op0=ALU.mult, op1=ALU.mult)\
                  .then_inc(s_tce, 1)
            dve.wait_ge(s_y, 1)
            g["add_residual"](dve)

        n_am = 2 + 4 * (CH - 1)
        n_rm = 3

    return Attn0()


def layouts(inp):
    f = lambda n: np.asarray(inp[n])
    out = {}

    def tiles_of_rows(w):
        pad = -w.shape[0] % P
        w = np.concatenate([w, np.zeros((pad, DIM), w.dtype)])
        return w.reshape(-1, P, KD, P).transpose(0, 3, 2, 1)

    out["x"] = f("L0_attn_hidden_states").reshape(NT, P, DIM).transpose(1, 0, 2)
    gates = {0: np.concatenate([f("L0_ffn_gate_w"), f("L0_ffn_shared_gate_w")]), 1: f("L1_ffn_gate_w")}
    gate = {0: np.concatenate([f("L0_ffn_expert_fc1").reshape(-1, DIM), f("L0_ffn_shared_fc1")]),
            1: f("L1_ffn_w_gate").reshape(-1, DIM)}
    up = {0: np.concatenate([f("L0_ffn_expert_fc2").reshape(-1, DIM), f("L0_ffn_shared_fc2")]),
          1: f("L1_ffn_w_up").reshape(-1, DIM)}
    down = {0: np.concatenate([f("L0_ffn_expert_proj").transpose(0, 2, 1).reshape(-1, DIM),
                               f("L0_ffn_shared_proj").transpose(1, 0)]),
            1: f("L1_ffn_w_down").transpose(0, 2, 1).reshape(-1, DIM)}
    for s in range(2):
        if f"ffn{s}" not in STAGES:
            continue
        E, K, F, S = MOE[s]
        NE, T = MOE_GATES[s], MOE_TILES[s]
        out[f"rw{s}"] = gates[s].reshape(NE, KD, P).transpose(2, 1, 0)
        out[f"w_gu{s}"] = np.stack([tiles_of_rows(gate[s]), tiles_of_rows(up[s])], 2).reshape(T, P, 2 * KD * P)
        d = np.concatenate([down[s], np.zeros((T * P - down[s].shape[0], DIM), down[s].dtype)])
        out[f"w_dn{s}"] = d.reshape(T, P, DIM)
        owner = np.minimum(np.arange(T * P) // F, NE - 1)
        sel = (owner[None, :] == np.arange(NE)[:, None])
        out[f"sel{s}"] = np.concatenate([sel] * PIECES).astype(mybir.dt.np(BF16))
        j, i = np.arange(E)[None, :], np.arange(E)[:, None]
        out[f"tri{s}"] = np.broadcast_to((j < i).astype(np.float32).reshape(-1), (P, E * E))
    p = np.arange(P)
    out["ident"] = np.eye(P, dtype=np.float32)
    out["identb"] = np.eye(P).astype(mybir.dt.np(BF16))
    same = p[:, None] // D0 == p[None, :] // D0
    out["headmask"] = same.astype(np.float32)
    out["causal_t"] = (p[:, None] <= p[None, :]).astype(np.float32)
    out["chunkmask"] = (same & (p[:, None] <= p[None, :])).astype(np.float32)
    if "attn1" in STAGES:
        inv = (1.0 / np.float32(THETA) ** (np.arange(0, DH, 2, dtype=np.float32) / np.float32(DH))).astype(np.float32)
        ang = np.outer(inv, np.arange(SEQ, dtype=np.float32)).astype(np.float32)
        out["cosT"] = np.concatenate([np.cos(ang)] * 2)
        out["sinT"] = np.concatenate([np.sin(ang), -np.sin(ang)])
        w = f("L1_attn_Wqkv")
        nq, nkv = HQ * DH, HKV * DH
        heads = lambda a: a.reshape(KD, P, -1, DH)
        out["wq1"] = heads(w[:, :nq]).transpose(2, 1, 0, 3)
        kv = [heads(w[:, nq:nq + nkv]), heads(w[:, nq + nkv:])]
        out["wkv"] = np.stack([a.transpose(1, 2, 0, 3) for a in kv], 2)
        out["wo1"] = f("L1_attn_Wo").reshape(HQ, DH, DIM)
    if "attn0" in STAGES:
        ws = [f("L0_attn_Wk"), f("L0_attn_Wq"), f("L0_attn_Wv"), np.repeat(f("L0_attn_Wb"), D0, axis=1),
              f("L0_attn_Wg")]
        out["w0"] = np.stack(ws).reshape(5, KD, P, DIM).transpose(2, 0, 1, 3)
        out["wo0"] = f("L0_attn_Wo").reshape(KD, P, DIM).transpose(1, 0, 2)
        cw = np.stack([f("L0_attn_conv_wk"), f("L0_attn_conv_wq"), f("L0_attn_conv_wv")])
        out["conv_w"] = cw.reshape(3, KD, P, CONV).transpose(2, 0, 1, 3)
        out["norm_w"] = np.tile(f("L0_attn_norm_w"), HH)[:, None]
    return {n: np.ascontiguousarray(a) for n, a in out.items()}


def kernel(**inputs):
    import concourse.bacc as _bacc
    from concourse.bass_utils import run_bass_kernel_spmd as _run

    nc = _bacc.Bacc("TRN2", target_bir_lowering=False, num_devices=1)
    arrays = layouts(inputs)
    io = {n: nc.dram_tensor(f"in_{n}", a.shape, mybir.dt.from_np(a.dtype), kind="ExternalInput").ap()
          for n, a in arrays.items()}
    io["out"] = nc.dram_tensor("out_x", (P, NT, DIM), F32, kind="ExternalOutput").ap()
    build(nc, io)
    r = _run(nc, [{f"in_{n}": a for n, a in arrays.items()}], core_ids=[0])
    got = r.results[0]["out_x"]
    return got.transpose(1, 0, 2).reshape(BATCH, SEQ, DIM)
```
